# Optimizing a Trainium2 kernel written in Bass

```python
import numpy as np
import jax
import jax.numpy as jnp

def _softmax(x, axis=-1):
    return jax.nn.softmax(x, axis=axis)

def _gelu(x):
    return jax.nn.gelu(x, approximate=True)

def _silu(x):
    return jax.nn.silu(x)

def _sigmoid(x):
    return jax.nn.sigmoid(x)

def _layernorm(x, axis=-1, eps=1e-05):
    m = jnp.mean(x, axis=axis, keepdims=True)
    v = jnp.var(x, axis=axis, keepdims=True)
    return (x - m) / jnp.sqrt(v + eps)

def _scatter_add(tgt, idx, src, axis=0):
    return tgt.at[idx].add(src)

def _segment_sum(src, seg, n):
    return jax.ops.segment_sum(src, seg, n)
kernel_name = 'mk_gnn_preln_d1_gnn_r64_6bac23'

def setup_inputs(seed: int=0):
    np.random.seed(seed)
    _w = jnp.asarray

    def _rec_inputs():
        import jax
        import jax.numpy as jnp
        _gk = jax.random.key(seed)
        x = -0.0009044 + 1 * jax.random.normal(jax.random.fold_in(_gk, 1), (100000, 32), jnp.float32)
        src = jax.random.randint(jax.random.fold_in(_gk, 2), (25000,), 0, 100000, jnp.int32)
        dst = jnp.minimum((100000 * jax.random.uniform(jax.random.fold_in(_gk, 3), (25000,)) ** 2.0).astype(jnp.int32), 99999)
        _o = jnp.argsort(dst, stable=True)
        src = src[_o]
        dst = dst[_o]
        edge_attr_2 = -5.09086e-05 + 0.577461 * jax.random.normal(jax.random.fold_in(_gk, 11), (25000, 2), jnp.float32)
        return (x, src, dst, edge_attr_2)
    x, src, dst, edge_attr_2 = _rec_inputs()

    def _L0_gnn_setup():
        import jax, jax.numpy as jnp
        import numpy as np
        N_NODES = 50000
        N_EDGES = 25000
        F_IN = 32
        F_OUT = 32
        BASIS = (4, 4)

        def _tent_basis(u, n):
            centers = jnp.linspace(-1.0, 1.0, n, dtype=u.dtype)
            h = 2.0 / (n - 1)
            return jnp.maximum(0.0, 1.0 - jnp.abs(u[:, None] - centers[None, :]) / h)
        key = jax.random.key(seed)
        k1, k2, k3, k4, k5 = jax.random.split(key, 5)
        x = jax.random.normal(k1, (N_NODES, F_IN), dtype=jnp.float32)
        edge_attr = jax.random.uniform(k2, (N_EDGES, 2), dtype=jnp.float32, minval=-1.0, maxval=1.0)
        weight = jax.random.uniform(k3, (*BASIS, F_IN, F_OUT), dtype=jnp.float32, minval=-0.05, maxval=0.05)
        src = jax.random.randint(k4, (N_EDGES,), 0, N_NODES)
        tgt = jax.random.randint(k5, (N_EDGES,), 0, N_NODES)
        edge_index = jnp.stack([tgt, src], axis=0).astype(jnp.int64)
        return {'x': x, 'edge_attr': edge_attr, 'weight': weight, 'edge_index': edge_index}
    _L0_gnn_all = _L0_gnn_setup()
    _L0_gnn_in = {k: v for k, v in _L0_gnn_all.items() if k in ('weight',)}
    del _L0_gnn_all
    return {'x': x, 'src': src, 'dst': dst, 'edge_attr_2': edge_attr_2, 'L0_gnn_weight': _L0_gnn_in['weight']}

def reference(x, src, dst, edge_attr_2, L0_gnn_weight):
    import jax
    import jax.numpy as jnp

    def _L0_gnn_ref(x, edge_attr, weight, edge_index):
        import jax, jax.numpy as jnp
        import numpy as np
        N_NODES = 50000
        N_EDGES = 25000
        F_IN = 32
        F_OUT = 32
        BASIS = (4, 4)

        def _tent_basis(u, n):
            centers = jnp.linspace(-1.0, 1.0, n, dtype=u.dtype)
            h = 2.0 / (n - 1)
            return jnp.maximum(0.0, 1.0 - jnp.abs(u[:, None] - centers[None, :]) / h)
        k1, k2, f_in, f_out = weight.shape
        n_nodes = x.shape[0]
        bu = _tent_basis(edge_attr[:, 0], k1)
        bv = _tent_basis(edge_attr[:, 1], k2)
        basis = (bu[:, :, None] * bv[:, None, :]).reshape(-1, k1 * k2)
        xj = x[edge_index[1]]
        w2 = weight.reshape(k1 * k2, f_in, f_out)
        msg = basis[:, 0:1] * (xj @ w2[0])
        for k in range(1, k1 * k2):
            msg = msg + basis[:, k:k + 1] * (xj @ w2[k])
        out = jax.ops.segment_sum(msg, edge_index[0], num_segments=n_nodes)
        return out
    edge_index = jnp.stack([src, dst])
    h = jnp.maximum(_layernorm(x, axis=-1), 0.0)
    x = x + _L0_gnn_ref(h, edge_attr_2, L0_gnn_weight, edge_index)
    return x

_drawn_inputs = setup_inputs


def setup_inputs(seed=0):
    import zlib

    import numpy as np

    out = dict(_drawn_inputs(seed))
    spreads = {}
    factors = {}
    for name, (base, spread) in spreads.items():
        noise = np.random.default_rng([zlib.crc32(name.encode()), seed]).standard_normal(out[name].shape)
        drawn = base * np.exp(spread * noise) if base else spread * noise
        out[name] = jnp.asarray(drawn.astype(out[name].dtype))
    for name, factor in factors.items():
        out[name] = (out[name] * factor).astype(out[name].dtype)
    return out
```

```python
from contextlib import ExitStack

import concourse.bass as bass
from concourse import mybir

P = 128
ALU = mybir.AluOpType
ACT = mybir.ActivationFunctionType
F32 = mybir.dt.float32
BF16 = mybir.dt.bfloat16
I32 = mybir.dt.int32
AX_X = mybir.AxisListType.X

BT = 4
PAIRS = BT // 2
SLOTS = 7
TURN = 2
JOIN = 3
STORE = 4
EPS = 1e-5
FAR = 9.0
LATER = float(1 << 20)


def gnn_kernel(nc, x, src, dst, edge_attr, weight, out):
    nodes, f = x.shape
    edges = src.shape[0]
    n_u, n_v = weight.shape[0], weight.shape[1]
    nk = n_u * n_v
    step_bt = BT * SLOTS
    tiles = -(-edges // (P * step_bt)) * step_bt
    batches = tiles // BT
    full_rows, tail = edges // tiles, edges % tiles
    assert full_rows == P - 1 and 0 < tail < tiles and f == 32 and nk * f == 512
    rounds = (batches - STORE) // SLOTS
    scale = (n_u - 1) / 2.0
    assert n_u == n_v

    with ExitStack() as ctx:
        def sb(name, shape, dt):
            return ctx.enter_context(nc.sbuf_tensor(name, shape, dt))

        def psum(name, shape, dt):
            return ctx.enter_context(nc.psum_tensor(name, shape, dt))

        def sem(name):
            return ctx.enter_context(nc.semaphore(name))

        dst_i = sb("dst_i", [P, tiles + step_bt], I32)
        src_i = sb("src_i", [P, tiles], I32)
        attr = sb("attr", [P, tiles, 2], F32)
        w_f = sb("w_f", [P, nk * f], F32)
        x_low = sb("x_low", [P, 2, f], F32)
        zero_f = sb("zero_f", [P, 2, P], F32)
        ident = sb("ident", [P, 2, P], BF16)
        later = sb("later", [P, P], BF16)
        dump_i = sb("dump_i", [P, 2], I32)
        column_i = sb("column_i", [P, P], I32)
        column = sb("column", [P, P], F32)
        dump = sb("dump", [P, 2], F32)
        center = sb("center", [P, n_u], F32)
        eps = sb("eps", [P, 1], F32)
        one = sb("one", [P, 1], F32)
        w_hi = sb("w_hi", [P, nk * f], BF16)
        w_r1 = sb("w_r1", [P, nk * f], F32)
        w_mid = sb("w_mid", [P, nk * f], BF16)
        w_lo = sb("w_lo", [P, nk * f], BF16)
        w_main = sb("w_main", [P, nk * f], BF16)
        w_rest = sb("w_rest", [P, nk * f], BF16)
        dist = sb("dist", [P, tiles, 2, n_u], F32)
        tent = sb("tent", [P, tiles, 2, n_u], F32)
        basis = sb("basis", [P, tiles, nk], F32)
        node_f = sb("node_f", [P, tiles], F32)
        node_neg = sb("node_neg", [P, tiles], F32)
        node_dump = sb("node_dump", [P, tiles], F32)
        node_off = sb("node_off", [P, tiles], F32)
        is_low = sb("is_low", [P, tiles, 2], F32)
        in_high = sb("in_high", [P, tiles], F32)
        node_row = sb("node_row", [P, tiles], F32)
        node_hi = sb("node_hi", [P, tiles], BF16)
        node_lo = sb("node_lo", [P, tiles], BF16)
        gath_idx = sb("gath_idx", [P, SLOTS * BT], I32)
        gath = sb("gath", [P, SLOTS * BT, f], F32)
        row_sum = sb("row_sum", [P, BT], F32)
        cen = sb("cen", [P, BT, f], F32)
        cen_sq = sb("cen_sq", [P, BT, f], F32)
        sq_sum = sb("sq_sum", [P, BT], F32)
        std = sb("std", [P, BT], F32)
        rstd = sb("rstd", [P, BT], F32)
        h = sb("h", [P, BT, f], F32)
        h_r1 = sb("h_r1", [P, BT, f], F32)
        h_parts = sb("h_parts", [P, SLOTS, BT, 4, f], BF16)
        hT = sb("hT", [P, SLOTS, BT * P], BF16)
        weighed = sb("weighed", [P, BT, nk, f], F32)
        msg = sb("msg", [P, tiles, f], F32)
        gap = sb("gap", [P, PAIRS, 3 * P], BF16)
        same = sb("same", [P, PAIRS, 3 * P], F32)
        low_hot = sb("low_hot", [P, BT, P], F32)
        low_msg = sb("low_msg", [P, BT, 2, f], F32)
        count = sb("count", [P, BT], F32)
        kept = sb("kept", [P, BT], F32)
        scat_idx = sb("scat_idx", [P, SLOTS * BT], I32)
        scat = sb("scat", [P, SLOTS * BT, f], F32)
        low_out = sb("low_out", [P, 2, f], F32)

        numbers = [psum(f"numbers{j}", [P, 3 * P], F32) for j in range(PAIRS)]
        hT_ps = psum("hT_ps", [P, BT * P], BF16)
        prod = [psum(f"prod{j}", [P, nk * f], F32) for j in range(2)]
        summed = psum("summed", [P, BT * f], F32)
        low = psum("low", [P, 2 * f], F32)

        s_pad = sem("s_pad")
        s_dst = sem("s_dst")
        s_src = sem("s_src")
        s_attr = sem("s_attr")
        s_w = sem("s_w")
        s_xlow = sem("s_xlow")
        s_copied = sem("s_copied")
        s_zero = sem("s_zero")
        s_ident = sem("s_ident")
        s_later = sem("s_later")
        s_part = sem("s_part")
        s_const = sem("s_const")
        s_column = sem("s_column")
        s_dump = sem("s_dump")
        s_node = sem("s_node")
        s_nodehi = sem("s_nodehi")
        s_nodelo = sem("s_nodelo")
        s_nodeneg = sem("s_nodeneg")
        s_nodeoff = sem("s_nodeoff")
        s_rowform = sem("s_rowform")
        s_whi = sem("s_whi")
        s_wr1 = sem("s_wr1")
        s_wmid = sem("s_wmid")
        s_wlo = sem("s_wlo")
        s_wready = sem("s_wready")
        s_dist = sem("s_dist")
        s_tent = sem("s_tent")
        s_basis = sem("s_basis")
        s_gidx = sem("s_gidx")
        s_gath = [sem(f"s_gath{g}") for g in range(SLOTS)]
        s_sum = sem("s_sum")
        s_cen = sem("s_cen")
        s_sq = sem("s_sq")
        s_var = sem("s_var")
        s_std = sem("s_std")
        s_rstd = sem("s_rstd")
        s_h = sem("s_h")
        s_hhi = sem("s_hhi")
        s_r1 = sem("s_r1")
        s_hmid = sem("s_hmid")
        s_hlo = sem("s_hlo")
        s_turned = sem("s_turned")
        s_hT = sem("s_hT")
        s_prod = sem("s_prod")
        s_weigh = sem("s_weigh")
        s_msg = sem("s_msg")
        s_numbers = sem("s_numbers")
        s_gap = sem("s_gap")
        s_same = sem("s_same")
        s_lowhot = sem("s_lowhot")
        s_lowmsg = sem("s_lowmsg")
        s_kept = sem("s_kept")
        s_sidx = sem("s_sidx")
        s_comb = sem("s_comb")
        s_scat_in = sem("s_scat_in")
        s_low = sem("s_low")
        s_scat = sem("s_scat")
        s_turns = sem("s_turns")
        s_out = sem("s_out")

        def tl(m, t=0, n=1):
            return bass.ds(m * BT + t, n)

        def steps(eng, step):
            for s in range(STORE):
                step(s, s, 0)
            with eng.Fori(0, rounds) as r:
                for k in range(SLOTS):
                    step(SLOTS * r + STORE + k, STORE + k, r)
            for s in range(STORE + SLOTS * rounds, batches + STORE):
                step(s, s, 0)

        block = ctx.enter_context(nc.Block())

        @block.sync
        def _(sp):
            def load(to, from_, width, s):
                cut = full_rows // 16 * 16
                sp.dma_start(to[0:cut], from_[0:cut * tiles * width].rearrange("(p t) -> p t", t=tiles * width)).then_inc(s, 16)
                sp.dma_start(to[cut:full_rows], from_[cut * tiles * width:full_rows * tiles * width]
                             .rearrange("(p t) -> p t", t=tiles * width)).then_inc(s, 16)
                sp.dma_start(to[full_rows:P, 0:tail * width], from_[full_rows * tiles * width:edges * width]
                             .rearrange("(p t) -> p t", p=1)).then_inc(s, 16)
            sp.wait_ge(s_pad, 4)
            load(dst_i[:, 0:tiles], dst, 1, s_dst)
            load(attr[:, :, :].rearrange("p t c -> p (t c)"), edge_attr.rearrange("e c -> (e c)"), 2, s_attr)
            load(src_i, src, 1, s_src)
            for g in range(4):
                sp.dma_start(w_f[g * f:(g + 1) * f, :].rearrange("i (k o) -> i k o", o=f),
                             weight.rearrange("a b i o -> i (a b) o")).then_inc(s_w, 16)
            sp.dma_start(x_low[:, :, :], x[0:2 * P, :].rearrange("(c p) f -> p c f", p=P)).then_inc(s_xlow, 16)
            rows = 800
            sp.dma_start(out.rearrange("(a b) c -> a (b c)", a=rows),
                         x.rearrange("(a b) c -> a (b c)", a=rows)).then_inc(s_copied, 16)
            sp.wait_ge(s_low, 1)
            sp.wait_ge(s_scat, 16 * tiles)
            sp.dma_start(out[0:2 * P, :].rearrange("(c p) f -> p c f", p=P), low_out[:, :, :]).then_inc(s_out, 16)
            sp.wait_ge(s_out, 16)

        @block.gpsimd
        def _(pool):
            bound = pool.to_reg(nodes - 1)
            pool.memset(zero_f[:, :, :], 0.0).then_inc(s_zero, 1)
            pool.iota(dump_i[:, :], pattern=[[P, 2]], base=0, channel_multiplier=1).then_inc(s_part, 1)
            pool.iota(column_i[:, :], pattern=[[1, P]], base=0, channel_multiplier=0).then_inc(s_part, 1)
            pool.wait_ge(s_zero, 1)
            pool.affine_select(out=ident[:, :, :], in_=zero_f[:, :, :], compare_op=ALU.not_equal, fill=1.0, base=0,
                               pattern=[[0, 2], [-1, P]], channel_multiplier=1).then_inc(s_ident, 1)
            pool.affine_select(out=later[:, :], in_=zero_f[:, 0, :], compare_op=ALU.is_ge, fill=LATER, base=0,
                               pattern=[[-1, P]], channel_multiplier=1).then_inc(s_later, 1)

            def gather(m, g, ts):
                pool.wait_ge(s_gidx, m + 1)
                pool.sem_inc(s_turns, 1)
                for t in ts:
                    c = g * BT + t
                    pool.indirect_dma_start(gath[:, c, :], None, x, bass.IndirectOffsetOnAxis(gath_idx[:, c:c + 1], 0),
                                            bounds_check=bound, oob_is_err=True).then_inc(s_gath[g], 16)

            def add_pair(d, g, j):
                pool.wait_ge(s_scat_in, d + 1)
                pool.wait_ge(s_sidx, d + 1)
                pool.sem_inc(s_turns, 1)
                for t in (2 * j, 2 * j + 1):
                    c = g * BT + t
                    pool.indirect_dma_start(out, bass.IndirectOffsetOnAxis(scat_idx[:, c:c + 1], 0), scat[:, c, :], None,
                                            bounds_check=bound, oob_is_err=True,
                                            compute_op=ALU.add).then_inc(s_scat, 16)

            def landed(d, j):
                pool.wait_ge(s_scat, (d * PAIRS + j + 1) * 32)

            for g in range(SLOTS):
                gather(g, g, range(BT))
            pool.wait_ge(s_copied, 16)
            with pool.Fori(0, batches // SLOTS - 1) as r:
                for g in range(SLOTS):
                    for j in range(PAIRS):
                        add_pair(SLOTS * r + g, g, j)
                        gather(SLOTS * r + SLOTS + g, g, (2 * j, 2 * j + 1))
                        landed(SLOTS * r + g, j)
            for g in range(SLOTS):
                for j in range(PAIRS):
                    add_pair(batches - SLOTS + g, g, j)
                    landed(batches - SLOTS + g, j)

        @block.scalar
        def _(act):
            act.wait_ge(s_dst, 48)
            act.copy(gath_idx[:, :], dst_i[:, 0:step_bt]).then_inc(s_gidx, SLOTS)
            act.wait_ge(s_const, 3)
            act.wait_ge(s_attr, 48)
            for c in range(n_u):
                act.activation(dist[:, :, :, c], attr[:, :, :], ACT.Abs, bias=center[:, c:c + 1]).then_inc(s_dist, 1)
            act.wait_ge(s_dist, n_u)
            act.activation(tent[:, :, :, :], dist[:, :, :, :], ACT.Relu, bias=one[:, 0:1],
                           scale=-scale).then_inc(s_tent, 1)
            act.wait_ge(s_w, 64)
            act.copy(w_hi[:, :], w_f[:, :]).then_inc(s_whi, 1)
            act.wait_ge(s_wr1, 1)
            act.copy(w_mid[:, :], w_r1[:, :]).then_inc(s_wmid, 1)
            act.wait_ge(s_whi, 1)
            act.copy(w_main[0:3 * f, :], w_hi[0:3 * f, :]).then_inc(s_wready, 1)
            act.wait_ge(s_wmid, 1)
            act.copy(w_main[3 * f:P, :], w_mid[3 * f:P, :]).then_inc(s_wready, 1)
            act.copy(w_rest[f:2 * f, :], w_mid[f:2 * f, :]).then_inc(s_wready, 1)
            act.wait_ge(s_wlo, 1)
            act.copy(w_rest[0:f, :], w_lo[0:f, :]).then_inc(s_wready, 1)

            def gaps(d):
                act.wait_ge(s_nodeneg, 1)
                for j in range(PAIRS):
                    act.wait_ge(s_numbers, PAIRS * d + j + 1)
                    for b in range(2):
                        act.activation(gap[:, j, P * b:P * (2 * b + 1)], numbers[j][:, P * b:P * (2 * b + 1)], ACT.Abs,
                                       bias=node_neg[:, tl(d, 2 * j + b)]).then_inc(s_gap, 1)

            def equal(d, j):
                for b in range(2):
                    act.wait_ge(s_gap, BT * d + 2 * j + b + 1)
                    act.activation(same[:, j, P * b:P * (2 * b + 1)], gap[:, j, P * b:P * (2 * b + 1)], ACT.Relu,
                                   bias=one[:, 0:1], scale=-1.0,
                                   accum_out=count[:, 2 * j + b:2 * j + b + 1]).then_inc(s_same, 1)

            def step(s, at, r):
                norm, join = at < batches, 0 <= at - JOIN < batches
                if 0 <= at - TURN < batches:
                    act.wait_ge(s_turned, s - TURN + 1)
                    act.copy(hT[:, (at - TURN) % SLOTS, :], hT_ps[:, :]).then_inc(s_hT, 1)
                if 0 <= at - STORE < batches:
                    g = (at - STORE) % SLOTS
                    act.wait_ge(s_comb, s - STORE + 1)
                    act.copy(scat[:, g * BT:(g + 1) * BT, :].rearrange("p t o -> p (t o)"),
                             summed[:, :]).then_inc(s_scat_in, 1)
                if norm:
                    g = at % SLOTS
                    act.wait_ge(s_var, s + 1)
                    act.activation(std[:, :], sq_sum[:, :], ACT.Sqrt, bias=eps[:, 0:1],
                                   scale=1.0 / f).then_inc(s_std, 1)
                    act.copy(gath_idx[:, g * BT:(g + 1) * BT], dst_i[:, tl(s + SLOTS, 0, BT)]).then_inc(s_gidx, 1)
                if join:
                    gaps(s - JOIN)
                if norm:
                    act.wait_ge(s_h, s + 1)
                    act.copy(h_parts[:, g, :, 0, :], h[:, :, :]).then_inc(s_hhi, 1)
                    act.copy(h_parts[:, g, :, 3, :], h[:, :, :]).then_inc(s_hhi, 1)
                if join:
                    act.wait_ge(s_comb, s - JOIN)
                    act.wait_ge(s_kept, s - JOIN)
                    equal(s - JOIN, 0)
                if norm:
                    act.wait_ge(s_r1, s + 1)
                    act.copy(h_parts[:, g, :, 1, :], h_r1[:, :, :]).then_inc(s_hmid, 1)
                if join:
                    equal(s - JOIN, 1)

            steps(act, step)

        @block.tensor
        def _(pe):
            blocks = [b[:, :].rearrange("p (c n) -> p c n", n=P) for b in numbers]
            pe.wait_ge(s_zero, 1)
            pe.matmul(low[:, :], zero_f[:, 0, :], zero_f[:, 0, 0:2 * f], start=True, stop=False, skip_group_check=True)
            pe.wait_ge(s_ident, 1)
            pe.wait_ge(s_later, 1)

            def turn(m, g):
                pe.wait_ge(s_hhi, 2 * m + 2)
                pe.wait_ge(s_hmid, m + 1)
                pe.wait_ge(s_hlo, m + 1)
                pe.wait_ge(s_hT, m)
                for t in range(BT):
                    mm = pe.transpose(hT_ps[:, t * P:(t + 1) * P],
                                      h_parts[:, g, t, :, :].rearrange("p c i -> p (c i)"), ident[:, 0, :])
                mm.then_inc(s_turned, 1)

            def products(m, g, first):
                pe.wait_ge(s_hT, m + 1)
                for t in range(BT):
                    if not (first and t < 2):
                        pe.wait_ge(s_weigh, BT * m + t - 1)
                    h_t = hT[:, g, t * P:(t + 1) * P]
                    pe.matmul(prod[t % 2][:, :], h_t, w_main[:, :], start=True, stop=False)
                    pe.matmul(prod[t % 2][:, :], h_t[0:2 * f, :], w_rest[0:2 * f, :], start=False,
                              stop=True).then_inc(s_prod, 1)

            def number_rows(d, first):
                for j in range(PAIRS):
                    if not first:
                        pe.wait_ge(s_gap, BT * (d - 1) + 2 * j + 2)
                    v = blocks[j]
                    for n, part in enumerate((node_hi, node_lo)):
                        pe.matmul(v[:, 0:2, :], part[:, tl(d, 2 * j)].to_broadcast([P, P]), ident[:, :, :],
                                  start=(n == 0), stop=False, skip_group_check=True)
                    pe.matmul(v[:, 0, :], ident[:, 0, :], later[:, :], start=False, stop=True, skip_group_check=True)
                    for n, part in enumerate((node_hi, node_lo)):
                        pe.matmul(v[:, 2, :], part[:, tl(d, 2 * j + 1)].to_broadcast([P, P]), ident[:, 0, :],
                                  start=(n == 0), stop=False, skip_group_check=True)
                    pe.matmul(v[:, 2, :], ident[:, 0, :], later[:, :], start=False, stop=True,
                              skip_group_check=True).then_inc(s_numbers, 1)

            def combine(d):
                pe.wait_ge(s_msg, BT * (d + 1))
                pe.wait_ge(s_same, BT * (d + 1))
                pe.wait_ge(s_scat_in, d)
                pe.wait_ge(s_lowhot, d + 1)
                pe.wait_ge(s_lowmsg, d + 1)
                for j in range(PAIRS):
                    a, b = msg[:, tl(d, 2 * j), :], msg[:, tl(d, 2 * j + 1), :]
                    a, b = a.rearrange("p t o -> p (t o)"), b.rearrange("p t o -> p (t o)")
                    to = [summed[:, (2 * j + c) * f:(2 * j + c + 1) * f] for c in range(2)]

                    def eq(c):
                        return same[:, j, c * P:(c + 1) * P]
                    pe.matmul(to[0], eq(0), a, start=True, stop=False)
                    pe.matmul(to[0], eq(1), b, start=False, stop=True)
                    pe.matmul(to[1], eq(2), b, start=True, stop=True)
                for t in range(BT):
                    mm = pe.matmul(low[:, :], low_hot[:, t, :], low_msg[:, t, :, :].rearrange("p c o -> p (c o)"),
                                   start=False, stop=False, skip_group_check=True)
                mm.then_inc(s_comb, 1)

            def step(s, at, r):
                if 0 <= at - TURN < batches:
                    turn(s - TURN, (at - TURN) % SLOTS)
                if 0 <= at - JOIN < batches:
                    if at == JOIN:
                        pe.wait_ge(s_nodelo, 1)
                    number_rows(s - JOIN, at == JOIN)
                if 0 <= at - TURN < batches:
                    if at == TURN:
                        pe.wait_ge(s_wready, 4)
                    products(s - TURN, (at - TURN) % SLOTS, at == TURN)
                if 0 <= at - JOIN < batches:
                    combine(s - JOIN)

            steps(pe, step)

        @block.vector
        def _(dve):
            dve.memset(dst_i[P - f:P, 0:tiles], 0).then_inc(s_pad, 1)
            dve.memset(dst_i[:, tiles:], 0).then_inc(s_pad, 1)
            dve.memset(src_i[P - f:P, :], 0).then_inc(s_pad, 1)
            dve.memset(attr[P - f:P, :, :], FAR).then_inc(s_pad, 1)
            for c in range(n_u):
                k = dve.memset(center[:, c:c + 1], 1.0 - 2.0 * c / (n_u - 1))
            k.then_inc(s_const, 1)
            dve.memset(eps[:, :], EPS).then_inc(s_const, 1)
            dve.memset(one[:, :], 1.0).then_inc(s_const, 1)
            dve.wait_ge(s_part, 2)
            dve.tensor_copy(dump[:, :], dump_i[:, :]).then_inc(s_dump, 1)
            dve.tensor_copy(column[:, :], column_i[:, :]).then_inc(s_column, 1)
            dve.wait_ge(s_tent, 1)
            dve.tensor_tensor(basis[:, :, :].rearrange("p t (a b) -> p t a b", b=n_v),
                              tent[:, :, 0, :].unsqueeze(3).to_broadcast([P, tiles, n_u, n_v]),
                              tent[:, :, 1, :].unsqueeze(2).to_broadcast([P, tiles, n_u, n_v]),
                              ALU.mult).then_inc(s_basis, 1)
            dve.wait_ge(s_whi, 1)
            dve.tensor_tensor(w_r1[:, :], w_f[:, :], w_hi[:, :], ALU.subtract).then_inc(s_wr1, 1)
            dve.wait_ge(s_src, 48)
            dve.tensor_copy(node_f[:, :], src_i[:, :]).then_inc(s_node, 1)
            dve.wait_ge(s_wmid, 1)
            dve.tensor_tensor(w_lo[:, :], w_r1[:, :], w_mid[:, :], ALU.subtract).then_inc(s_wlo, 1)
            dve.wait_ge(s_node, 1)
            dve.tensor_copy(node_hi[:, :], node_f[:, :]).then_inc(s_nodehi, 1)
            dve.tensor_scalar(node_neg[:, :], node_f[:, :], -1.0, None, ALU.mult).then_inc(s_nodeneg, 1)
            dve.tensor_scalar(in_high[:, :], node_f[:, :], float(P), None, ALU.is_ge).then_inc(s_rowform, 1)
            dve.tensor_scalar(is_low[:, :, 0], node_f[:, :], float(P), None, ALU.is_lt).then_inc(s_rowform, 1)
            dve.wait_ge(s_dump, 1)
            dve.tensor_tensor(node_dump[:, :].rearrange("p (j b) -> p j b", b=2), node_f[:, :].rearrange("p (j b) -> p j b", b=2),
                              dump[:, :].unsqueeze(1).to_broadcast([P, tiles // 2, 2]), ALU.subtract).then_inc(s_rowform, 1)
            dve.wait_ge(s_rowform, 3)
            dve.scalar_tensor_tensor(out=node_row[:, :], in0=in_high[:, :], scalar=-float(P), in1=node_f[:, :],
                                     op0=ALU.mult, op1=ALU.add).then_inc(s_rowform, 1)
            dve.scalar_tensor_tensor(out=is_low[:, :, 1], in0=node_f[:, :], scalar=2.0 * P, in1=in_high[:, :],
                                     op0=ALU.is_lt, op1=ALU.mult).then_inc(s_rowform, 1)
            dve.scalar_tensor_tensor(out=node_off[:, :], in0=node_f[:, :], scalar=2.0 * P, in1=node_dump[:, :],
                                     op0=ALU.is_ge, op1=ALU.mult).then_inc(s_nodeoff, 1)
            dve.wait_ge(s_nodehi, 1)
            dve.tensor_tensor(node_lo[:, :], node_f[:, :], node_hi[:, :], ALU.subtract).then_inc(s_nodelo, 1)

            def weigh(m, t, first):
                if not first:
                    dve.wait_ge(s_msg, BT * (m - 1) + t + 1)
                dve.wait_ge(s_prod, BT * m + t + 1)
                dve.tensor_tensor(weighed[:, t, :, :], prod[t % 2][:, :].rearrange("p (k o) -> p k o", o=f),
                                  basis[:, tl(m, t), :].rearrange("p t k -> p (t k)").unsqueeze(2).to_broadcast([P, nk, f]),
                                  ALU.mult).then_inc(s_weigh, 1)

            def message(m, t):
                dve.wait_ge(s_weigh, BT * m + t + 1)
                dve.tensor_reduce(msg[:, tl(m, t), :].rearrange("p t o -> p (t o)"),
                                  weighed[:, t, :, :].rearrange("p k o -> p o k"), AX_X, ALU.add).then_inc(s_msg, 1)

            def step(s, at, r):
                norm, turn, join = at < batches, 0 <= at - TURN < batches, 0 <= at - JOIN < batches
                m, g = s - TURN, at % SLOTS
                d, gd = s - JOIN, (at - JOIN) % SLOTS
                if at == TURN:
                    dve.wait_ge(s_basis, 1)

                def spread(t):
                    return t[:, :].unsqueeze(2).to_broadcast([P, BT, f])
                if turn:
                    weigh(m, 0, at == TURN)
                if norm:
                    dve.wait_ge(s_gath[g], 16 * BT * (r + at // SLOTS + 1))
                    rows = gath[:, g * BT:(g + 1) * BT, :]
                    dve.tensor_reduce(row_sum[:, :], rows, AX_X, ALU.add).then_inc(s_sum, 1)
                if turn:
                    weigh(m, 1, at == TURN)
                if norm:
                    dve.wait_ge(s_sum, s + 1)
                    dve.scalar_tensor_tensor(out=cen[:, :, :], in0=spread(row_sum), scalar=-1.0 / f, in1=rows,
                                             op0=ALU.mult, op1=ALU.add).then_inc(s_cen, 1)
                if join:
                    if at == JOIN:
                        dve.wait_ge(s_rowform, 5)
                        dve.wait_ge(s_column, 1)
                    dve.wait_ge(s_comb, d)
                    dve.tensor_tensor(low_hot[:, :, :], column[:, :].unsqueeze(1).to_broadcast([P, BT, P]),
                                      node_row[:, tl(d, 0, BT)].unsqueeze(2).to_broadcast([P, BT, P]),
                                      ALU.is_equal).then_inc(s_lowhot, 1)
                if turn:
                    message(m, 0)
                if norm:
                    dve.wait_ge(s_cen, s + 1)
                    dve.tensor_tensor(cen_sq[:, :, :], cen[:, :, :], cen[:, :, :], ALU.mult).then_inc(s_sq, 1)
                if turn:
                    weigh(m, 2, at == TURN)
                if norm:
                    dve.wait_ge(s_sq, s + 1)
                    dve.tensor_reduce(sq_sum[:, :], cen_sq[:, :, :], AX_X, ALU.add).then_inc(s_var, 1)
                if turn:
                    message(m, 1)
                    weigh(m, 3, at == TURN)
                if norm:
                    dve.wait_ge(s_std, s + 1)
                    dve.reciprocal(rstd[:, :], std[:, :]).then_inc(s_rstd, 1)
                if join:
                    dve.wait_ge(s_msg, BT * (d + 1))
                    dve.tensor_tensor(low_msg[:, :, :, :], msg[:, tl(d, 0, BT), :].unsqueeze(2).to_broadcast([P, BT, 2, f]),
                                      is_low[:, tl(d, 0, BT), :].unsqueeze(3).to_broadcast([P, BT, 2, f]),
                                      ALU.mult).then_inc(s_lowmsg, 1)
                if turn:
                    message(m, 2)
                if norm:
                    dve.wait_ge(s_rstd, s + 1)
                    dve.scalar_tensor_tensor(out=h[:, :, :], in0=cen[:, :, :], scalar=0.0, in1=spread(rstd),
                                             op0=ALU.max, op1=ALU.mult).then_inc(s_h, 1)
                if turn:
                    message(m, 3)
                if norm:
                    dve.wait_ge(s_hhi, 2 * s + 2)
                    dve.wait_ge(s_hlo, s)
                    dve.tensor_tensor(h_r1[:, :, :], h[:, :, :], h_parts[:, g, :, 0, :], ALU.subtract).then_inc(s_r1, 1)
                if join:
                    dve.wait_ge(s_same, BT * (d + 1))
                    dve.wait_ge(s_sidx, d)
                    dve.scalar_tensor_tensor(out=kept[:, :], in0=count[:, :], scalar=1.0, in1=node_off[:, tl(d, 0, BT)],
                                             op0=ALU.is_equal, op1=ALU.mult).then_inc(s_kept, 1)
                    dve.wait_ge(s_kept, d + 1)
                    dve.tensor_tensor(scat_idx[:, gd * BT:(gd + 1) * BT].rearrange("p (j b) -> p j b", b=2),
                                      kept[:, :].rearrange("p (j b) -> p j b", b=2),
                                      dump[:, :].unsqueeze(1).to_broadcast([P, PAIRS, 2]), ALU.add).then_inc(s_sidx, 1)
                if norm:
                    dve.wait_ge(s_hmid, s + 1)
                    dve.tensor_tensor(h_parts[:, g, :, 2, :], h_r1[:, :, :], h_parts[:, g, :, 1, :],
                                      ALU.subtract).then_inc(s_hlo, 1)

            steps(dve, step)
            dve.wait_ge(s_xlow, 16)
            dve.wait_ge(s_comb, batches)
            dve.tensor_tensor(low_out[:, :, :], low[:, :].rearrange("p (c o) -> p c o", c=2), x_low[:, :, :], ALU.add).then_inc(s_low, 1)


_INS = ["x", "src", "dst", "edge_attr_2", "L0_gnn_weight"]


def kernel(**inputs):
    import numpy as np
    import concourse.bacc as bacc
    from concourse.bass_utils import run_bass_kernel_spmd

    nc = bacc.Bacc("TRN2", target_bir_lowering=False, num_devices=1)
    arrays, args = {}, []
    for name in _INS:
        a = np.ascontiguousarray(inputs[name])
        arrays[f"in_{name}"] = a
        args.append(nc.dram_tensor(f"in_{name}", a.shape, mybir.dt.from_np(a.dtype), kind="ExternalInput").ap())
    shape = arrays["in_x"].shape
    args.append(nc.dram_tensor("out", shape, F32, kind="ExternalOutput").ap())
    gnn_kernel(nc, *args)
    r = run_bass_kernel_spmd(nc, [arrays], core_ids=[0])
    return r.results[0]["out"]
```

```python
from contextlib import ExitStack

import concourse.bass as bass
from concourse import mybir

P = 128
ALU = mybir.AluOpType
ACT = mybir.ActivationFunctionType
F32 = mybir.dt.float32
BF16 = mybir.dt.bfloat16
I32 = mybir.dt.int32
AX_X = mybir.AxisListType.X

BT = 4
PAIRS = BT // 2
SLOTS = 7
TURN = 1
WEIGH = 2
NUMBER = 2
JOIN = 3
COMBINE = 4
STORE = 5
PIECES = 10
EPS = 1e-5
FAR = 9.0
LATER = float(1 << 20)


def gnn_kernel(nc, x, src, dst, edge_attr, weight, out):
    nodes, f = x.shape
    edges = src.shape[0]
    n_u, n_v = weight.shape[0], weight.shape[1]
    nk = n_u * n_v
    step_bt = BT * SLOTS
    tiles = -(-edges // (P * step_bt)) * step_bt
    batches = tiles // BT
    full_rows, tail = edges // tiles, edges % tiles
    assert full_rows == P - 1 and 0 < tail < tiles and f == 32 and nk * f == 512
    rounds = (batches - STORE) // SLOTS
    scale = (n_u - 1) / 2.0
    assert n_u == n_v

    with ExitStack() as ctx:
        def sb(name, shape, dt):
            return ctx.enter_context(nc.sbuf_tensor(name, shape, dt))

        def psum(name, shape, dt):
            return ctx.enter_context(nc.psum_tensor(name, shape, dt))

        def sem(name):
            return ctx.enter_context(nc.semaphore(name))

        dst_i = sb("dst_i", [P, tiles + step_bt], I32)
        src_i = sb("src_i", [P, tiles], I32)
        attr = sb("attr", [P, tiles, 2], F32)
        w_f = sb("w_f", [P, nk * f], F32)
        x_low = sb("x_low", [P, 2, f], F32)
        zero_f = sb("zero_f", [P, 2, P], F32)
        ident = sb("ident", [P, 2, P], BF16)
        later = sb("later", [P, P], BF16)
        dump_i = sb("dump_i", [P, 2], I32)
        column_i = sb("column_i", [P, P], I32)
        column = sb("column", [P, P], F32)
        dump = sb("dump", [P, 2], F32)
        center = sb("center", [P, n_u], F32)
        eps = sb("eps", [P, 1], F32)
        one = sb("one", [P, 1], F32)
        w_hi = sb("w_hi", [P, nk * f], BF16)
        w_r1 = sb("w_r1", [P, nk * f], F32)
        w_mid = sb("w_mid", [P, nk * f], BF16)
        w_lo = sb("w_lo", [P, nk * f], BF16)
        w_main = sb("w_main", [P, nk * f], BF16)
        w_rest = sb("w_rest", [P, nk * f], BF16)
        dist = sb("dist", [P, tiles, 2, n_u], F32)
        tent = sb("tent", [P, tiles, 2, n_u], F32)
        basis = sb("basis", [P, tiles, nk], F32)
        node_f = sb("node_f", [P, tiles], F32)
        node_neg = sb("node_neg", [P, tiles], F32)
        node_dump = sb("node_dump", [P, tiles], F32)
        node_off = sb("node_off", [P, tiles], F32)
        is_low = sb("is_low", [P, tiles, 2], F32)
        in_high = sb("in_high", [P, tiles], F32)
        node_row = sb("node_row", [P, tiles], F32)
        node_hi = sb("node_hi", [P, tiles], BF16)
        node_lo = sb("node_lo", [P, tiles], BF16)
        gath_idx = sb("gath_idx", [P, SLOTS * BT], I32)
        gath = sb("gath", [P, SLOTS * BT, f], F32)
        row_sum = sb("row_sum", [P, BT], F32)
        cen = sb("cen", [P, BT, f], F32)
        cen_sq = sb("cen_sq", [P, BT, f], F32)
        sq_sum = sb("sq_sum", [P, BT], F32)
        std = sb("std", [P, BT], F32)
        rstd = sb("rstd", [P, BT], F32)
        h = sb("h", [P, BT, f], F32)
        h_r1 = sb("h_r1", [P, BT, f], F32)
        h_parts = sb("h_parts", [P, SLOTS, BT, 4, f], BF16)
        hT = sb("hT", [P, SLOTS, BT * P], BF16)
        weighed = sb("weighed", [P, BT, nk, f], F32)
        msg = sb("msg", [P, tiles, f], F32)
        gap = sb("gap", [P, PAIRS, 3 * P], BF16)
        same = sb("same", [P, SLOTS, PAIRS, 3 * P], F32)
        low_hot = sb("low_hot", [P, SLOTS, BT, P], F32)
        low_msg = sb("low_msg", [P, SLOTS, BT, 2, f], F32)
        count = sb("count", [P, BT], F32)
        kept = sb("kept", [P, BT], F32)
        scat_idx = sb("scat_idx", [P, SLOTS * BT], I32)
        scat = sb("scat", [P, SLOTS * BT, f], F32)
        low_out = sb("low_out", [P, 2, f], F32)

        numbers = [psum(f"numbers{j}", [P, 3 * P], F32) for j in range(PAIRS)]
        hT_ps = psum("hT_ps", [P, BT * P], BF16)
        prod = [psum(f"prod{j}", [P, nk * f], F32) for j in range(2)]
        summed = psum("summed", [P, BT * f], F32)
        low = psum("low", [P, 2 * f], F32)

        s_pad = sem("s_pad")
        s_dst = sem("s_dst")
        s_src = sem("s_src")
        s_attr = sem("s_attr")
        s_w = sem("s_w")
        s_xlow = sem("s_xlow")
        s_copied = sem("s_copied")
        s_zero = sem("s_zero")
        s_ident = sem("s_ident")
        s_later = sem("s_later")
        s_part = sem("s_part")
        s_const = sem("s_const")
        s_column = sem("s_column")
        s_dump = sem("s_dump")
        s_node = sem("s_node")
        s_nodehi = sem("s_nodehi")
        s_nodelo = sem("s_nodelo")
        s_nodeneg = sem("s_nodeneg")
        s_nodeoff = sem("s_nodeoff")
        s_rowform = sem("s_rowform")
        s_whi = sem("s_whi")
        s_wr1 = sem("s_wr1")
        s_wmid = sem("s_wmid")
        s_wlo = sem("s_wlo")
        s_wready = sem("s_wready")
        s_dist = sem("s_dist")
        s_tent = sem("s_tent")
        s_basis = sem("s_basis")
        s_gidx = sem("s_gidx")
        s_gath = [sem(f"s_gath{g}") for g in range(SLOTS)]
        s_sum = sem("s_sum")
        s_cen = sem("s_cen")
        s_sq = sem("s_sq")
        s_var = sem("s_var")
        s_std = sem("s_std")
        s_rstd = sem("s_rstd")
        s_h = sem("s_h")
        s_hhi = sem("s_hhi")
        s_r1 = sem("s_r1")
        s_hmid = sem("s_hmid")
        s_hlo = sem("s_hlo")
        s_turned = sem("s_turned")
        s_hT = sem("s_hT")
        s_prod = sem("s_prod")
        s_weigh = sem("s_weigh")
        s_msg = sem("s_msg")
        s_numbers = sem("s_numbers")
        s_gap = sem("s_gap")
        s_same = sem("s_same")
        s_lowhot = sem("s_lowhot")
        s_lowmsg = sem("s_lowmsg")
        s_kept = sem("s_kept")
        s_sidx = sem("s_sidx")
        s_comb = sem("s_comb")
        s_scat_in = sem("s_scat_in")
        s_low = sem("s_low")
        s_low_out = sem("s_low_out")
        s_scat = sem("s_scat")
        s_turns = sem("s_turns")
        s_out = sem("s_out")

        def tl(m, t=0, n=1):
            return bass.ds(m * BT + t, n)

        def steps(eng, step):
            for s in range(STORE):
                step(s, s, 0)
            with eng.Fori(0, rounds) as r:
                for k in range(SLOTS):
                    step(SLOTS * r + STORE + k, STORE + k, r)
            for s in range(STORE + SLOTS * rounds, batches + STORE):
                step(s, s, 0)

        block = ctx.enter_context(nc.Block())

        @block.sync
        def _(sp):
            def load(to, from_, width, s):
                cut = full_rows // 16 * 16
                sp.dma_start(to[0:cut], from_[0:cut * tiles * width].rearrange("(p t) -> p t", t=tiles * width)).then_inc(s, 16)
                sp.dma_start(to[cut:full_rows], from_[cut * tiles * width:full_rows * tiles * width]
                             .rearrange("(p t) -> p t", t=tiles * width)).then_inc(s, 16)
                sp.dma_start(to[full_rows:P, 0:tail * width], from_[full_rows * tiles * width:edges * width]
                             .rearrange("(p t) -> p t", p=1)).then_inc(s, 16)
            sp.wait_ge(s_pad, 4)
            load(dst_i[:, 0:tiles], dst, 1, s_dst)
            load(attr[:, :, :].rearrange("p t c -> p (t c)"), edge_attr.rearrange("e c -> (e c)"), 2, s_attr)
            load(src_i, src, 1, s_src)
            for g in range(4):
                sp.dma_start(w_f[g * f:(g + 1) * f, :].rearrange("i (k o) -> i k o", o=f),
                             weight.rearrange("a b i o -> i (a b) o")).then_inc(s_w, 16)
            sp.dma_start(x_low[:, :, :], x[0:2 * P, :].rearrange("(c p) f -> p c f", p=P)).then_inc(s_xlow, 16)
            rows = nodes // PIECES
            for n in range(PIECES):
                sp.dma_start(out[n * rows:(n + 1) * rows, :].rearrange("(a b) c -> a (b c)", a=16 * 5),
                             x[n * rows:(n + 1) * rows, :].rearrange("(a b) c -> a (b c)", a=16 * 5)).then_inc(s_copied, 16)
            sp.wait_ge(s_low_out, 1)
            sp.wait_ge(s_scat, 16 * tiles)
            sp.dma_start(out[0:2 * P, :].rearrange("(c p) f -> p c f", p=P), low_out[:, :, :]).then_inc(s_out, 16)
            sp.wait_ge(s_out, 16)

        @block.gpsimd
        def _(pool):
            bound = pool.to_reg(nodes - 1)
            pool.memset(zero_f[:, :, :], 0.0).then_inc(s_zero, 1)
            pool.iota(dump_i[:, :], pattern=[[P, 2]], base=0, channel_multiplier=1).then_inc(s_part, 1)
            pool.iota(column_i[:, :], pattern=[[1, P]], base=0, channel_multiplier=0).then_inc(s_part, 1)
            pool.wait_ge(s_zero, 1)
            pool.affine_select(out=ident[:, :, :], in_=zero_f[:, :, :], compare_op=ALU.not_equal, fill=1.0, base=0,
                               pattern=[[0, 2], [-1, P]], channel_multiplier=1).then_inc(s_ident, 1)
            pool.affine_select(out=later[:, :], in_=zero_f[:, 0, :], compare_op=ALU.is_ge, fill=LATER, base=0,
                               pattern=[[-1, P]], channel_multiplier=1).then_inc(s_later, 1)

            def gather(m, g, ts):
                pool.wait_ge(s_gidx, m + 1)
                pool.sem_inc(s_turns, 1)
                for t in ts:
                    c = g * BT + t
                    pool.indirect_dma_start(gath[:, c, :], None, x, bass.IndirectOffsetOnAxis(gath_idx[:, c:c + 1], 0),
                                            bounds_check=bound, oob_is_err=True).then_inc(s_gath[g], 16)

            def add_pair(d, g, j):
                pool.wait_ge(s_scat_in, d + 1)
                pool.wait_ge(s_sidx, d + 1)
                pool.sem_inc(s_turns, 1)
                for t in (2 * j, 2 * j + 1):
                    c = g * BT + t
                    pool.indirect_dma_start(out, bass.IndirectOffsetOnAxis(scat_idx[:, c:c + 1], 0), scat[:, c, :], None,
                                            bounds_check=bound, oob_is_err=True,
                                            compute_op=ALU.add).then_inc(s_scat, 16)

            def landed(d, j):
                pool.wait_ge(s_scat, (d * PAIRS + j + 1) * 32)

            for g in range(SLOTS):
                gather(g, g, range(BT))
            pool.wait_ge(s_copied, 16 * PIECES)
            with pool.Fori(0, batches // SLOTS - 1) as r:
                for g in range(SLOTS):
                    for j in range(PAIRS):
                        add_pair(SLOTS * r + g, g, j)
                        gather(SLOTS * r + SLOTS + g, g, (2 * j, 2 * j + 1))
                        landed(SLOTS * r + g, j)
            for g in range(SLOTS):
                for j in range(PAIRS):
                    add_pair(batches - SLOTS + g, g, j)
                    landed(batches - SLOTS + g, j)

        @block.scalar
        def _(act):
            act.wait_ge(s_dst, 48)
            act.copy(gath_idx[:, :], dst_i[:, 0:step_bt]).then_inc(s_gidx, SLOTS)
            act.wait_ge(s_const, 3)
            act.wait_ge(s_attr, 48)
            for c in range(n_u):
                act.activation(dist[:, :, :, c], attr[:, :, :], ACT.Abs, bias=center[:, c:c + 1]).then_inc(s_dist, 1)
            act.wait_ge(s_dist, n_u)
            act.activation(tent[:, :, :, :], dist[:, :, :, :], ACT.Relu, bias=one[:, 0:1],
                           scale=-scale).then_inc(s_tent, 1)
            act.wait_ge(s_w, 64)
            act.copy(w_hi[:, :], w_f[:, :]).then_inc(s_whi, 1)
            act.wait_ge(s_wr1, 1)
            act.copy(w_mid[:, :], w_r1[:, :]).then_inc(s_wmid, 1)
            act.wait_ge(s_whi, 1)
            act.copy(w_main[0:3 * f, :], w_hi[0:3 * f, :]).then_inc(s_wready, 1)
            act.wait_ge(s_wmid, 1)
            act.copy(w_main[3 * f:P, :], w_mid[3 * f:P, :]).then_inc(s_wready, 1)
            act.copy(w_rest[f:2 * f, :], w_mid[f:2 * f, :]).then_inc(s_wready, 1)
            act.wait_ge(s_wlo, 1)
            act.copy(w_rest[0:f, :], w_lo[0:f, :]).then_inc(s_wready, 1)

            def gaps(d, first):
                if first:
                    act.wait_ge(s_nodeneg, 1)
                else:
                    act.wait_ge(s_same, BT * d)
                for j in range(PAIRS):
                    act.wait_ge(s_numbers, PAIRS * d + j + 1)
                    for b in range(2):
                        act.activation(gap[:, j, P * b:P * (2 * b + 1)], numbers[j][:, P * b:P * (2 * b + 1)], ACT.Abs,
                                       bias=node_neg[:, tl(d, 2 * j + b)]).then_inc(s_gap, 1)

            def equal(d, gd, j):
                for b in range(2):
                    act.wait_ge(s_gap, BT * d + 2 * j + b + 1)
                    act.activation(same[:, gd, j, P * b:P * (2 * b + 1)], gap[:, j, P * b:P * (2 * b + 1)], ACT.Relu,
                                   bias=one[:, 0:1], scale=-1.0,
                                   accum_out=count[:, 2 * j + b:2 * j + b + 1]).then_inc(s_same, 1)

            def step(s, at, r):
                norm, join, d = at < batches, 0 <= at - JOIN < batches, s - JOIN
                gd = (at - JOIN) % SLOTS
                if 0 <= at - STORE < batches:
                    g = (at - STORE) % SLOTS
                    act.wait_ge(s_comb, PAIRS * (s - STORE + 1))
                    act.copy(scat[:, g * BT:(g + 1) * BT, :].rearrange("p t o -> p (t o)"),
                             summed[:, :]).then_inc(s_scat_in, 1)
                if join:
                    gaps(d, at == JOIN)
                if 0 <= at - TURN < batches:
                    act.wait_ge(s_turned, s - TURN + 1)
                    act.copy(hT[:, (at - TURN) % SLOTS, :], hT_ps[:, :]).then_inc(s_hT, 1)
                if norm:
                    g = at % SLOTS
                    act.wait_ge(s_var, s + 1)
                    act.activation(std[:, :], sq_sum[:, :], ACT.Sqrt, bias=eps[:, 0:1],
                                   scale=1.0 / f).then_inc(s_std, 1)
                    act.copy(gath_idx[:, g * BT:(g + 1) * BT], dst_i[:, tl(s + SLOTS, 0, BT)]).then_inc(s_gidx, 1)
                if join:
                    if at > JOIN:
                        act.wait_ge(s_kept, d)
                    equal(d, gd, 0)
                if norm:
                    act.wait_ge(s_h, s + 1)
                    act.copy(h_parts[:, g, :, 0, :], h[:, :, :]).then_inc(s_hhi, 1)
                    act.copy(h_parts[:, g, :, 3, :], h[:, :, :]).then_inc(s_hhi, 1)
                if join:
                    equal(d, gd, 1)
                if norm:
                    act.wait_ge(s_r1, s + 1)
                    act.copy(h_parts[:, g, :, 1, :], h_r1[:, :, :]).then_inc(s_hmid, 1)

            steps(act, step)

        @block.tensor
        def _(pe):
            blocks = [b[:, :].rearrange("p (c n) -> p c n", n=P) for b in numbers]
            pe.wait_ge(s_zero, 1)
            pe.matmul(low[:, :], zero_f[:, 0, :], zero_f[:, 0, 0:2 * f], start=True, stop=False, skip_group_check=True)
            pe.wait_ge(s_ident, 1)
            pe.wait_ge(s_later, 1)

            def turn(m, g, first):
                pe.wait_ge(s_hhi, 2 * m + 2)
                pe.wait_ge(s_hmid, m + 1)
                pe.wait_ge(s_hlo, m + 1)
                if not first:
                    pe.wait_ge(s_hT, m)
                for t in range(BT):
                    mm = pe.transpose(hT_ps[:, t * P:(t + 1) * P],
                                      h_parts[:, g, t, :, :].rearrange("p c i -> p (c i)"), ident[:, 0, :])
                mm.then_inc(s_turned, 1)

            def products(m, g, ts, first):
                pe.wait_ge(s_hT, m + 1)
                for t in ts:
                    if not first:
                        pe.wait_ge(s_weigh, BT * m + t - 1)
                    h_t = hT[:, g, t * P:(t + 1) * P]
                    pe.matmul(prod[t % 2][:, :], h_t, w_main[:, :], start=True, stop=False)
                    pe.matmul(prod[t % 2][:, :], h_t[0:2 * f, :], w_rest[0:2 * f, :], start=False,
                              stop=True).then_inc(s_prod, 1)

            def number_rows(d, first):
                for j in range(PAIRS):
                    if first:
                        pe.wait_ge(s_nodelo, 1)
                    else:
                        pe.wait_ge(s_gap, BT * (d - 1) + 2 * j + 2)
                    v = blocks[j]
                    for n, part in enumerate((node_hi, node_lo)):
                        pe.matmul(v[:, 0:2, :], part[:, tl(d, 2 * j)].to_broadcast([P, P]), ident[:, :, :],
                                  start=(n == 0), stop=False, skip_group_check=True)
                    pe.matmul(v[:, 0, :], ident[:, 0, :], later[:, :], start=False, stop=True, skip_group_check=True)
                    for n, part in enumerate((node_hi, node_lo)):
                        pe.matmul(v[:, 2, :], part[:, tl(d, 2 * j + 1)].to_broadcast([P, P]), ident[:, 0, :],
                                  start=(n == 0), stop=False, skip_group_check=True)
                    pe.matmul(v[:, 2, :], ident[:, 0, :], later[:, :], start=False, stop=True,
                              skip_group_check=True).then_inc(s_numbers, 1)

            def combine(d, g, j, first):
                if j == 0:
                    pe.wait_ge(s_same, BT * (d + 1))
                    pe.wait_ge(s_msg, BT * (d + 1))
                    if not first:
                        pe.wait_ge(s_scat_in, d)
                a, b = (msg[:, tl(d, 2 * j + c), :].rearrange("p t o -> p (t o)") for c in range(2))
                to = [summed[:, (2 * j + c) * f:(2 * j + c + 1) * f] for c in range(2)]
                eq = [same[:, g, j, c * P:(c + 1) * P] for c in range(3)]
                pe.matmul(to[0], eq[0], a, start=True, stop=False)
                pe.matmul(to[0], eq[1], b, start=False, stop=True)
                pe.matmul(to[1], eq[2], b, start=True, stop=True).then_inc(s_comb, 1)

            def combine_low(d, g):
                pe.wait_ge(s_lowhot, d + 1)
                pe.wait_ge(s_lowmsg, d + 1)
                for t in range(BT):
                    mm = pe.matmul(low[:, :], low_hot[:, g, t, :], low_msg[:, g, t, :, :].rearrange("p c o -> p (c o)"),
                                   start=False, stop=False, skip_group_check=True)
                mm.then_inc(s_low, 1)

            def step(s, at, r):
                weighed_, combined = 0 <= at - WEIGH < batches, 0 <= at - COMBINE < batches
                m, gm, gc = s - WEIGH, (at - WEIGH) % SLOTS, (at - COMBINE) % SLOTS
                if at == WEIGH:
                    pe.wait_ge(s_wready, 4)
                if weighed_:
                    products(m, gm, (0, 1), at == WEIGH)
                if 0 <= at - TURN < batches:
                    turn(s - TURN, (at - TURN) % SLOTS, at == TURN)
                if combined:
                    combine(s - COMBINE, gc, 0, at == COMBINE)
                if weighed_:
                    products(m, gm, (2,), False)
                if combined:
                    combine(s - COMBINE, gc, 1, False)
                if weighed_:
                    products(m, gm, (3,), False)
                if combined:
                    combine_low(s - COMBINE, gc)
                if 0 <= at - NUMBER < batches:
                    number_rows(s - NUMBER, at == NUMBER)

            steps(pe, step)

        @block.vector
        def _(dve):
            dve.memset(dst_i[P - f:P, 0:tiles], 0).then_inc(s_pad, 1)
            dve.memset(dst_i[:, tiles:], 0).then_inc(s_pad, 1)
            dve.memset(src_i[P - f:P, :], 0).then_inc(s_pad, 1)
            dve.memset(attr[P - f:P, :, :], FAR).then_inc(s_pad, 1)
            for c in range(n_u):
                k = dve.memset(center[:, c:c + 1], 1.0 - 2.0 * c / (n_u - 1))
            k.then_inc(s_const, 1)
            dve.memset(eps[:, :], EPS).then_inc(s_const, 1)
            dve.memset(one[:, :], 1.0).then_inc(s_const, 1)
            dve.wait_ge(s_part, 2)
            dve.tensor_copy(dump[:, :], dump_i[:, :]).then_inc(s_dump, 1)
            dve.tensor_copy(column[:, :], column_i[:, :]).then_inc(s_column, 1)
            dve.wait_ge(s_tent, 1)
            dve.tensor_tensor(basis[:, :, :].rearrange("p t (a b) -> p t a b", b=n_v),
                              tent[:, :, 0, :].unsqueeze(3).to_broadcast([P, tiles, n_u, n_v]),
                              tent[:, :, 1, :].unsqueeze(2).to_broadcast([P, tiles, n_u, n_v]),
                              ALU.mult).then_inc(s_basis, 1)
            dve.wait_ge(s_whi, 1)
            dve.tensor_tensor(w_r1[:, :], w_f[:, :], w_hi[:, :], ALU.subtract).then_inc(s_wr1, 1)
            dve.wait_ge(s_src, 48)
            dve.tensor_copy(node_f[:, :], src_i[:, :]).then_inc(s_node, 1)
            dve.wait_ge(s_wmid, 1)
            dve.tensor_tensor(w_lo[:, :], w_r1[:, :], w_mid[:, :], ALU.subtract).then_inc(s_wlo, 1)
            dve.wait_ge(s_node, 1)
            dve.tensor_copy(node_hi[:, :], node_f[:, :]).then_inc(s_nodehi, 1)
            dve.tensor_scalar(node_neg[:, :], node_f[:, :], -1.0, None, ALU.mult).then_inc(s_nodeneg, 1)
            dve.tensor_scalar(in_high[:, :], node_f[:, :], float(P), None, ALU.is_ge).then_inc(s_rowform, 1)
            dve.tensor_scalar(is_low[:, :, 0], node_f[:, :], float(P), None, ALU.is_lt).then_inc(s_rowform, 1)
            dve.wait_ge(s_dump, 1)
            dve.tensor_tensor(node_dump[:, :].rearrange("p (j b) -> p j b", b=2), node_f[:, :].rearrange("p (j b) -> p j b", b=2),
                              dump[:, :].unsqueeze(1).to_broadcast([P, tiles // 2, 2]), ALU.subtract).then_inc(s_rowform, 1)
            dve.wait_ge(s_rowform, 3)
            dve.scalar_tensor_tensor(out=node_row[:, :], in0=in_high[:, :], scalar=-float(P), in1=node_f[:, :],
                                     op0=ALU.mult, op1=ALU.add).then_inc(s_rowform, 1)
            dve.scalar_tensor_tensor(out=is_low[:, :, 1], in0=node_f[:, :], scalar=2.0 * P, in1=in_high[:, :],
                                     op0=ALU.is_lt, op1=ALU.mult).then_inc(s_rowform, 1)
            dve.scalar_tensor_tensor(out=node_off[:, :], in0=node_f[:, :], scalar=2.0 * P, in1=node_dump[:, :],
                                     op0=ALU.is_ge, op1=ALU.mult).then_inc(s_nodeoff, 1)
            dve.wait_ge(s_nodehi, 1)
            dve.tensor_tensor(node_lo[:, :], node_f[:, :], node_hi[:, :], ALU.subtract).then_inc(s_nodelo, 1)

            def weigh(m, t, first):
                if not first:
                    dve.wait_ge(s_msg, BT * (m - 1) + t + 1)
                dve.wait_ge(s_prod, BT * m + t + 1)
                dve.tensor_tensor(weighed[:, t, :, :], prod[t % 2][:, :].rearrange("p (k o) -> p k o", o=f),
                                  basis[:, tl(m, t), :].rearrange("p t k -> p (t k)").unsqueeze(2).to_broadcast([P, nk, f]),
                                  ALU.mult).then_inc(s_weigh, 1)

            def message(m, t):
                dve.wait_ge(s_weigh, BT * m + t + 1)
                dve.tensor_reduce(msg[:, tl(m, t), :].rearrange("p t o -> p (t o)"),
                                  weighed[:, t, :, :].rearrange("p k o -> p o k"), AX_X, ALU.add).then_inc(s_msg, 1)

            def step(s, at, r):
                norm, turn, join = at < batches, 0 <= at - WEIGH < batches, 0 <= at - JOIN < batches
                m, g = s - WEIGH, at % SLOTS
                d, gd = s - JOIN, (at - JOIN) % SLOTS
                if at == WEIGH:
                    dve.wait_ge(s_basis, 1)

                def spread(t):
                    return t[:, :].unsqueeze(2).to_broadcast([P, BT, f])
                if turn:
                    weigh(m, 0, at == WEIGH)
                if norm:
                    dve.wait_ge(s_gath[g], 16 * BT * (r + at // SLOTS + 1))
                    rows = gath[:, g * BT:(g + 1) * BT, :]
                    dve.tensor_reduce(row_sum[:, :], rows, AX_X, ALU.add).then_inc(s_sum, 1)
                if turn:
                    weigh(m, 1, at == WEIGH)
                if norm:
                    dve.wait_ge(s_sum, s + 1)
                    dve.scalar_tensor_tensor(out=cen[:, :, :], in0=spread(row_sum), scalar=-1.0 / f, in1=rows,
                                             op0=ALU.mult, op1=ALU.add).then_inc(s_cen, 1)
                if join:
                    if at == JOIN:
                        dve.wait_ge(s_rowform, 5)
                        dve.wait_ge(s_column, 1)
                    dve.tensor_tensor(low_hot[:, gd, :, :], column[:, :].unsqueeze(1).to_broadcast([P, BT, P]),
                                      node_row[:, tl(d, 0, BT)].unsqueeze(2).to_broadcast([P, BT, P]),
                                      ALU.is_equal).then_inc(s_lowhot, 1)
                if turn:
                    message(m, 0)
                if norm:
                    dve.wait_ge(s_cen, s + 1)
                    dve.tensor_tensor(cen_sq[:, :, :], cen[:, :, :], cen[:, :, :], ALU.mult).then_inc(s_sq, 1)
                if turn:
                    weigh(m, 2, at == WEIGH)
                if norm:
                    dve.wait_ge(s_sq, s + 1)
                    dve.tensor_reduce(sq_sum[:, :], cen_sq[:, :, :], AX_X, ALU.add).then_inc(s_var, 1)
                if turn:
                    message(m, 1)
                    weigh(m, 3, at == WEIGH)
                if norm:
                    dve.wait_ge(s_std, s + 1)
                    dve.reciprocal(rstd[:, :], std[:, :]).then_inc(s_rstd, 1)
                if join:
                    dve.wait_ge(s_msg, BT * (d + 1))
                    dve.tensor_tensor(low_msg[:, gd, :, :, :], msg[:, tl(d, 0, BT), :].unsqueeze(2).to_broadcast([P, BT, 2, f]),
                                      is_low[:, tl(d, 0, BT), :].unsqueeze(3).to_broadcast([P, BT, 2, f]),
                                      ALU.mult).then_inc(s_lowmsg, 1)
                if turn:
                    message(m, 2)
                if norm:
                    dve.wait_ge(s_rstd, s + 1)
                    dve.scalar_tensor_tensor(out=h[:, :, :], in0=cen[:, :, :], scalar=0.0, in1=spread(rstd),
                                             op0=ALU.max, op1=ALU.mult).then_inc(s_h, 1)
                if turn:
                    message(m, 3)
                if norm:
                    dve.wait_ge(s_hhi, 2 * s + 2)
                    if at > 0:
                        dve.wait_ge(s_hlo, s)
                    dve.tensor_tensor(h_r1[:, :, :], h[:, :, :], h_parts[:, g, :, 0, :], ALU.subtract).then_inc(s_r1, 1)
                if join:
                    dve.wait_ge(s_same, BT * (d + 1))
                    if at > JOIN:
                        dve.wait_ge(s_sidx, d)
                    dve.scalar_tensor_tensor(out=kept[:, :], in0=count[:, :], scalar=1.0, in1=node_off[:, tl(d, 0, BT)],
                                             op0=ALU.is_equal, op1=ALU.mult).then_inc(s_kept, 1)
                    dve.wait_ge(s_kept, d + 1)
                    dve.tensor_tensor(scat_idx[:, gd * BT:(gd + 1) * BT].rearrange("p (j b) -> p j b", b=2),
                                      kept[:, :].rearrange("p (j b) -> p j b", b=2),
                                      dump[:, :].unsqueeze(1).to_broadcast([P, PAIRS, 2]), ALU.add).then_inc(s_sidx, 1)
                if norm:
                    dve.wait_ge(s_hmid, s + 1)
                    dve.tensor_tensor(h_parts[:, g, :, 2, :], h_r1[:, :, :], h_parts[:, g, :, 1, :],
                                      ALU.subtract).then_inc(s_hlo, 1)

            steps(dve, step)
            dve.wait_ge(s_xlow, 16)
            dve.wait_ge(s_low, batches)
            dve.tensor_tensor(low_out[:, :, :], low[:, :].rearrange("p (c o) -> p c o", c=2), x_low[:, :, :], ALU.add).then_inc(s_low_out, 1)


_INS = ["x", "src", "dst", "edge_attr_2", "L0_gnn_weight"]


def kernel(**inputs):
    import numpy as np
    import concourse.bacc as bacc
    from concourse.bass_utils import run_bass_kernel_spmd

    nc = bacc.Bacc("TRN2", target_bir_lowering=False, num_devices=1)
    arrays, args = {}, []
    for name in _INS:
        a = np.ascontiguousarray(inputs[name])
        arrays[f"in_{name}"] = a
        args.append(nc.dram_tensor(f"in_{name}", a.shape, mybir.dt.from_np(a.dtype), kind="ExternalInput").ap())
    shape = arrays["in_x"].shape
    args.append(nc.dram_tensor("out", shape, F32, kind="ExternalOutput").ap())
    gnn_kernel(nc, *args)
    r = run_bass_kernel_spmd(nc, [arrays], core_ids=[0])
    return r.results[0]["out"]
```

```python
from contextlib import ExitStack

import concourse.bass as bass
from concourse import mybir

P = 128
ALU = mybir.AluOpType
ACT = mybir.ActivationFunctionType
F32 = mybir.dt.float32
BF16 = mybir.dt.bfloat16
I32 = mybir.dt.int32
AX_X = mybir.AxisListType.X

BT = 4
BLOCKS = BT * (BT + 1) // 2
LOW = BT * P
SLOTS = 7
AHEAD = 3 * SLOTS
BEFORE_ADDS = AHEAD - 2
GATHERED = 2 * SLOTS
ADD_SLOTS = 22
COMPARE = 1
TURN = 1
WEIGH = 2
KEEP = 2
COMBINE = 3
PIECES = 10
EPS = 1e-5
FAR = 9.0
LATER = float(1 << 20)


def gnn_kernel(nc, x, src, dst, edge_attr, weight, out):
    nodes, f = x.shape
    edges = src.shape[0]
    n_u, n_v = weight.shape[0], weight.shape[1]
    step_bt = BT * SLOTS
    tiles = -(-edges // (P * step_bt)) * step_bt
    batches = tiles // BT
    full_rows, tail = edges // tiles, edges % tiles
    assert full_rows == P - 1 and step_bt <= tail < tiles and n_u * f == P and n_v * f * BT <= 512
    rounds = (batches - COMBINE) // SLOTS
    add_rounds = (batches - AHEAD) // GATHERED
    assert GATHERED % SLOTS == 0 and AHEAD + GATHERED * add_rounds == batches
    assert 1 + ADD_SLOTS * add_rounds <= batches
    scale = (n_u - 1) / 2.0
    assert n_u == n_v

    with ExitStack() as ctx:
        def sb(name, shape, dt):
            return ctx.enter_context(nc.sbuf_tensor(name, shape, dt))

        def psum(name, shape, dt):
            return ctx.enter_context(nc.psum_tensor(name, shape, dt))

        def sem(name):
            return ctx.enter_context(nc.semaphore(name))

        dst_i = sb("dst_i", [P, tiles + step_bt], I32)
        src_i = sb("src_i", [P, tiles], I32)
        attr = sb("attr", [P, tiles, 2], F32)
        w_ai = sb("w_ai", [P, n_v * f], F32)
        x_low = sb("x_low", [P, BT, f], F32)
        zero_f = sb("zero_f", [P, P], F32)
        ident_f = sb("ident_f", [P, P], F32)
        ident = sb("ident", [P, P], BF16)
        later = sb("later", [P, P], BF16)
        dump_i = sb("dump_i", [P, BT], I32)
        column_i = sb("column_i", [P, P], I32)
        column = sb("column", [P, P], F32)
        dump = sb("dump", [P, BT], F32)
        center = sb("center", [P, n_u], F32)
        eps = sb("eps", [P, 1], F32)
        one = sb("one", [P, 1], F32)
        dist = sb("dist", [P, tiles, 2, n_u], F32)
        tent = sb("tent", [P, tiles, 2, n_u], F32)
        node_f = sb("node_f", [P, tiles], F32)
        node_neg = sb("node_neg", [P, tiles], F32)
        node_dump = sb("node_dump", [P, tiles], F32)
        node_off = sb("node_off", [P, tiles], F32)
        past = sb("past", [P, tiles, BT + 1], F32)
        is_low = sb("is_low", [P, tiles, BT], F32)
        blocks_past = sb("blocks_past", [P, tiles], F32)
        node_row = sb("node_row", [P, tiles], F32)
        node_hi = sb("node_hi", [P, tiles], BF16)
        node_lo = sb("node_lo", [P, tiles], BF16)
        gath_idx = sb("gath_idx", [P, SLOTS * BT], I32)
        gath = sb("gath", [P, SLOTS * BT, f], F32)
        row_sum = sb("row_sum", [P, BT], F32)
        cen = sb("cen", [P, BT, f], F32)
        cen_sq = sb("cen_sq", [P, BT, f], F32)
        sq_sum = sb("sq_sum", [P, BT], F32)
        std = sb("std", [P, BT], F32)
        rstd = sb("rstd", [P, BT], F32)
        h = sb("h", [P, BT, f], F32)
        z = sb("z", [P, BT, n_u, f], F32)
        zT = sb("zT", [P, BT * P], F32)
        weighed = sb("weighed", [P, BT, n_v, f], F32)
        msg = sb("msg", [P, tiles, f], F32)
        gap = sb("gap", [P, BLOCKS * P], BF16)
        same = sb("same", [P, SLOTS, BLOCKS * P], F32)
        low_hot = sb("low_hot", [P, SLOTS, BT, P], F32)
        low_msg = sb("low_msg", [P, SLOTS, BT, BT, f], F32)
        count = sb("count", [P, BT], F32)
        kept = sb("kept", [P, BT], F32)
        scat_idx = sb("scat_idx", [P, ADD_SLOTS * BT], I32)
        scat = sb("scat", [P, ADD_SLOTS * BT, f], F32)
        low_out = sb("low_out", [P, BT, f], F32)

        banks = ((1,), (0, 2), (3,))
        numbers = [psum(f"numbers{b}", [P, sum(t + 1 for t in ts) * P], F32) for b, ts in enumerate(banks)]
        turns = [t for ts in banks for t in ts]
        zT_ps = psum("zT_ps", [P, BT * P], F32)
        prod = psum("prod", [P, BT * n_v * f], F32)
        summed = psum("summed", [P, BT * f], F32)
        low = psum("low", [P, BT * f], F32)

        s_pad = sem("s_pad")
        s_first = sem("s_first")
        s_dst = sem("s_dst")
        s_src = sem("s_src")
        s_attr = sem("s_attr")
        s_w = sem("s_w")
        s_xlow = sem("s_xlow")
        s_copied = [sem(f"s_copied{c}") for c in range(2)]
        s_zero = sem("s_zero")
        s_ident = sem("s_ident")
        s_later = sem("s_later")
        s_part = sem("s_part")
        s_const = sem("s_const")
        s_column = sem("s_column")
        s_dump = sem("s_dump")
        s_node = sem("s_node")
        s_nodehi = sem("s_nodehi")
        s_nodelo = sem("s_nodelo")
        s_nodeneg = sem("s_nodeneg")
        s_nodeoff = sem("s_nodeoff")
        s_rowform = sem("s_rowform")
        s_dist = sem("s_dist")
        s_tent = sem("s_tent")
        s_gidx = sem("s_gidx")
        s_gath = [sem(f"s_gath{g}") for g in range(SLOTS)]
        s_sum = sem("s_sum")
        s_cen = sem("s_cen")
        s_sq = sem("s_sq")
        s_var = sem("s_var")
        s_std = sem("s_std")
        s_rstd = sem("s_rstd")
        s_h = sem("s_h")
        s_z = sem("s_z")
        s_turned = sem("s_turned")
        s_zT = sem("s_zT")
        s_prod = sem("s_prod")
        s_weigh = sem("s_weigh")
        s_msg = sem("s_msg")
        s_numbers = sem("s_numbers")
        s_gap = sem("s_gap")
        s_same = sem("s_same")
        s_lowhot = sem("s_lowhot")
        s_lowmsg = sem("s_lowmsg")
        s_kept = sem("s_kept")
        s_sidx = sem("s_sidx")
        s_comb = sem("s_comb")
        s_scat_in = sem("s_scat_in")
        s_low = sem("s_low")
        s_low_out = sem("s_low_out")
        s_scat = sem("s_scat")
        s_turns = sem("s_turns")
        s_room = sem("s_room")
        s_out = sem("s_out")

        def section(t):
            return slice(t * (t + 1) // 2 * P, (t + 1) * (t + 2) // 2 * P)

        def tl(m, t=0, n=1):
            return bass.ds(m * BT + t, n)

        def steps(eng, step):
            for s in range(COMBINE):
                step(s, s, 0)
            with eng.Fori(0, rounds) as r:
                for k in range(SLOTS):
                    step(SLOTS * r + COMBINE + k, COMBINE + k, r)
            for s in range(COMBINE + SLOTS * rounds, batches + COMBINE):
                step(s, s, 0)

        def there(at, lag):
            return 0 <= at - lag < batches, at == lag

        block = ctx.enter_context(nc.Block())

        @block.sync
        def _(sp):
            def load(to, from_, width, s):
                cut = full_rows // 16 * 16
                run = tiles * width
                for p, q in ((0, cut), (cut, full_rows)):
                    sp.dma_start(to[p:q], from_[p * run:q * run].rearrange("(p t) -> p t", t=run)).then_inc(s, 16)
                sp.dma_start(to[full_rows:P, 0:tail * width],
                             from_[full_rows * run:edges * width].rearrange("(p t) -> p t", p=1)).then_inc(s, 16)
            sp.dma_start(gath_idx[:, :], bass.AP(dst.tensor, 0, [[tiles, P], [1, step_bt]])).then_inc(s_first, 16)
            sp.wait_ge(s_pad, 4)
            load(dst_i[:, 0:tiles], dst, 1, s_dst)
            load(attr[:, :, :].rearrange("p t c -> p (t c)"), edge_attr.rearrange("e c -> (e c)"), 2, s_attr)
            load(src_i, src, 1, s_src)
            for a in range(n_u):
                sp.dma_start(w_ai[a * f:(a + 1) * f, :].rearrange("i (b o) -> i b o", o=f),
                             weight[a].rearrange("b i o -> i b o")).then_inc(s_w, 16)
            sp.dma_start(x_low[:, :, :], x[0:LOW, :].rearrange("(c p) f -> p c f", p=P)).then_inc(s_xlow, 16)
            rows = nodes // PIECES
            for n in range(PIECES):
                if n >= 2:
                    sp.wait_ge(s_copied[n % 2], 16 * (n // 2))
                to, from_ = (t[n * rows:(n + 1) * rows, :].rearrange("(a b) c -> a (b c)", a=16 * 5)
                             for t in (out, x))
                sp.dma_start(to, from_).then_inc(s_copied[n % 2], 16)
            sp.wait_ge(s_low_out, 1)
            sp.wait_ge(s_scat, 16 * tiles)
            sp.dma_start(out[0:LOW, :].rearrange("(c p) f -> p c f", p=P), low_out[:, :, :]).then_inc(s_out, 16)
            sp.wait_ge(s_out, 16)

        @block.gpsimd
        def _(pool):
            bound = pool.to_reg(nodes - 1)
            pool.memset(zero_f[:, :], 0.0).then_inc(s_zero, 1)
            pool.iota(dump_i[:, :], pattern=[[P, BT]], base=0, channel_multiplier=1).then_inc(s_part, 1)
            pool.iota(column_i[:, :], pattern=[[1, P]], base=0, channel_multiplier=0).then_inc(s_part, 1)
            pool.wait_ge(s_zero, 1)
            pool.affine_select(out=ident[:, :], in_=zero_f[:, :], compare_op=ALU.not_equal, fill=1.0, base=0,
                               pattern=[[-1, P]], channel_multiplier=1).then_inc(s_ident, 1)
            pool.affine_select(out=later[:, :], in_=zero_f[:, :], compare_op=ALU.is_ge, fill=LATER, base=0,
                               pattern=[[-1, P]], channel_multiplier=1).then_inc(s_later, 1)

            pool.affine_select(out=ident_f[:, :], in_=zero_f[:, :], compare_op=ALU.not_equal, fill=1.0, base=0,
                               pattern=[[-1, P]], channel_multiplier=1).then_inc(s_ident, 1)

            def gather(m, g, ts, from_ring=True):
                if ts[0] == 0 and from_ring:
                    pool.wait_ge(s_gidx, m - SLOTS + 1)
                    pool.sem_inc(s_turns, 1)
                for t in ts:
                    c = g * BT + t
                    pool.indirect_dma_start(gath[:, c, :], None, x,
                                            bass.IndirectOffsetOnAxis(gath_idx[:, c:c + 1], 0),
                                            bounds_check=bound, oob_is_err=True).then_inc(s_gath[g], 16)

            def add(d, g):
                pool.wait_ge(s_scat_in, d + 1)
                pool.wait_ge(s_sidx, d + 1)
                pool.sem_inc(s_turns, 1)
                for t in range(BT):
                    c = g * BT + t
                    pool.indirect_dma_start(out, bass.IndirectOffsetOnAxis(scat_idx[:, c:c + 1], 0),
                                            scat[:, c, :], None,
                                            bounds_check=bound, oob_is_err=True,
                                            compute_op=ALU.add).then_inc(s_scat, 16)

            def landed(d):
                pool.wait_ge(s_scat, (d + 1) * 16 * BT)
                pool.sem_inc(s_room, 1)

            pool.sem_inc(s_room, ADD_SLOTS)
            pool.wait_ge(s_first, 16)
            pool.sem_inc(s_turns, 1)
            for m in range(BEFORE_ADDS):
                gather(m, m % SLOTS, range(BT), m >= SLOTS)
            for c in s_copied:
                pool.wait_ge(c, 16 * PIECES // 2)
            add(0, 0)
            gather(BEFORE_ADDS, BEFORE_ADDS % SLOTS, range(BT))
            landed(0)
            for m in range(BEFORE_ADDS + 1, AHEAD):
                gather(m, m % SLOTS, range(BT))
            gathered = GATHERED * BT
            with pool.Fori(0, add_rounds) as r:
                for g in range(ADD_SLOTS):
                    d = 1 + ADD_SLOTS * r + g
                    add(d, (1 + g) % ADD_SLOTS)
                    for t in range(g * gathered // ADD_SLOTS, (g + 1) * gathered // ADD_SLOTS):
                        gather(GATHERED * r + AHEAD + t // BT, t // BT % SLOTS, (t % BT,))
                    landed(d)
            for d in range(1 + ADD_SLOTS * add_rounds, batches):
                add(d, d % ADD_SLOTS)
                landed(d)

        @block.scalar
        def _(act):
            act.wait_ge(s_const, 3)
            act.wait_ge(s_attr, 48)
            for c in range(n_u):
                act.activation(dist[:, :, :, c], attr[:, :, :], ACT.Abs, bias=center[:, c:c + 1]).then_inc(s_dist, 1)
            act.wait_ge(s_dist, n_u)
            act.activation(tent[:, :, :, :], dist[:, :, :, :], ACT.Relu, bias=one[:, 0:1],
                           scale=-scale).then_inc(s_tent, 1)

            def gaps(d, first):
                if first:
                    act.wait_ge(s_nodeneg, 1)
                else:
                    act.wait_ge(s_same, BT * d)
                for b, ts in enumerate(banks):
                    act.wait_ge(s_numbers, len(banks) * d + b + 1)
                    c = 0
                    for t in ts:
                        act.activation(gap[:, section(t)], numbers[b][:, c:c + (t + 1) * P], ACT.Abs,
                                       bias=node_neg[:, tl(d, t)]).then_inc(s_gap, 1)
                        c += (t + 1) * P

            def equal(d, g):
                for n, t in enumerate(turns):
                    act.wait_ge(s_gap, BT * d + n + 1)
                    act.activation(same[:, g, section(t)], gap[:, section(t)], ACT.Relu, bias=one[:, 0:1], scale=-1.0,
                                   accum_out=count[:, t:t + 1]).then_inc(s_same, 1)

            def step(s, at, r):
                g = at % SLOTS
                combined, _ = there(at, COMBINE)
                if combined:
                    d = s - COMBINE
                    act.wait_ge(s_comb, d + 1)
                    act.wait_ge(s_room, d + 1)
                    act.copy(scat[:, bass.ds(d % ADD_SLOTS * BT, BT), :].rearrange("p t o -> p (t o)"),
                             summed[:, :]).then_inc(s_scat_in, 1)
                here, first = there(at, TURN)
                if here:
                    m = s - TURN
                    act.wait_ge(s_turned, m + 1)
                    if not first:
                        act.wait_ge(s_prod, m)
                    act.copy(zT[:, :], zT_ps[:, :]).then_inc(s_zT, 1)
                compared, first = there(at, COMPARE)
                if compared:
                    gaps(s - COMPARE, first)
                if at < batches:
                    act.wait_ge(s_var, s + 1)
                    act.activation(std[:, :], sq_sum[:, :], ACT.Sqrt, bias=eps[:, 0:1],
                                   scale=1.0 / f).then_inc(s_std, 1)
                    if at == 0:
                        act.wait_ge(s_dst, 48)
                    act.copy(gath_idx[:, g * BT:(g + 1) * BT], dst_i[:, tl(s + SLOTS, 0, BT)]).then_inc(s_gidx, 1)
                if compared:
                    if not first:
                        act.wait_ge(s_kept, s - COMPARE)
                    equal(s - COMPARE, (at - COMPARE) % SLOTS)

            steps(act, step)

        @block.tensor
        def _(pe):
            pe.wait_ge(s_zero, 1)
            pe.matmul(low[:, :], zero_f[:, :], zero_f[:, 0:BT * f], start=True, stop=False, skip_group_check=True)
            pe.wait_ge(s_ident, 2)
            pe.wait_ge(s_later, 1)

            def turn(m, first):
                pe.wait_ge(s_z, m + 1)
                if not first:
                    pe.wait_ge(s_zT, m)
                for t in range(BT):
                    mm = pe.transpose(zT_ps[:, t * P:(t + 1) * P], z[:, t, :, :].rearrange("p a i -> p (a i)"),
                                      ident_f[:, :])
                mm.then_inc(s_turned, 1)

            def products(m, first):
                pe.wait_ge(s_zT, m + 1)
                if first:
                    pe.wait_ge(s_w, 16 * n_u)
                else:
                    pe.wait_ge(s_weigh, m)
                for t in range(BT):
                    mm = pe.matmul(prod[:, t * n_v * f:(t + 1) * n_v * f], zT[:, t * P:(t + 1) * P], w_ai[:, :],
                                   start=True, stop=True)
                mm.then_inc(s_prod, 1)

            def number_rows(d, first):
                if first:
                    pe.wait_ge(s_nodelo, 1)
                for b, ts in enumerate(banks):
                    if not first:
                        pe.wait_ge(s_gap, BT * (d - 1) + sum(len(x) for x in banks[:b + 1]))
                    at = 0
                    for t in ts:
                        for c in range(t + 1):
                            to = numbers[b][:, at:at + P]
                            pe.matmul(to, node_hi[:, tl(d, c)].to_broadcast([P, P]), ident[:, :],
                                      start=True, stop=False, skip_group_check=True)
                            mm = pe.matmul(to, node_lo[:, tl(d, c)].to_broadcast([P, P]), ident[:, :],
                                           start=False, stop=(c < t), skip_group_check=True)
                            at += P
                        mm = pe.matmul(to, ident[:, :], later[:, :], start=False, stop=True, skip_group_check=True)
                    mm.then_inc(s_numbers, 1)

            def combine(d, g, first):
                pe.wait_ge(s_same, BT * (d + 1))
                pe.wait_ge(s_msg, d + 1)
                if not first:
                    pe.wait_ge(s_scat_in, d)
                for c in range(BT):
                    for t in range(c, BT):
                        at = section(t).start + c * P
                        mm = pe.matmul(summed[:, c * f:(c + 1) * f], same[:, g, at:at + P],
                                       msg[:, tl(d, t), :].rearrange("p t o -> p (t o)"),
                                       start=(t == c), stop=(t == BT - 1))
                mm.then_inc(s_comb, 1)

            def combine_low(d, g):
                pe.wait_ge(s_lowhot, d + 1)
                pe.wait_ge(s_lowmsg, d + 1)
                for t in range(BT):
                    mm = pe.matmul(low[:, :], low_hot[:, g, t, :],
                                   low_msg[:, g, t, :, :].rearrange("p c o -> p (c o)"),
                                   start=False, stop=False, skip_group_check=True)
                mm.then_inc(s_low, 1)

            def step(s, at, r):
                turned, first = there(at, TURN)
                combined, first_c = there(at, COMBINE)
                gc = (at - COMBINE) % SLOTS
                if combined:
                    combine(s - COMBINE, gc, first_c)
                if turned:
                    turn(s - TURN, first)
                if combined:
                    combine_low(s - COMBINE, gc)
                if turned:
                    products(s - TURN, first)
                if at < batches:
                    number_rows(s, at == 0)

            steps(pe, step)

        @block.vector
        def _(dve):
            dve.memset(dst_i[P - f:P, 0:tiles], 0).then_inc(s_pad, 1)
            dve.memset(dst_i[:, tiles:], 0).then_inc(s_pad, 1)
            dve.memset(src_i[P - f:P, :], 0).then_inc(s_pad, 1)
            dve.memset(attr[P - f:P, :, :], FAR).then_inc(s_pad, 1)
            for c in range(n_u):
                k = dve.memset(center[:, c:c + 1], 1.0 - 2.0 * c / (n_u - 1))
            k.then_inc(s_const, 1)
            dve.memset(eps[:, :], EPS).then_inc(s_const, 1)
            dve.memset(one[:, :], 1.0).then_inc(s_const, 1)
            dve.wait_ge(s_part, 2)
            dve.tensor_copy(dump[:, :], dump_i[:, :]).then_inc(s_dump, 1)
            dve.tensor_copy(column[:, :], column_i[:, :]).then_inc(s_column, 1)
            dve.wait_ge(s_src, 48)
            dve.tensor_copy(node_f[:, :], src_i[:, :]).then_inc(s_node, 1)
            dve.wait_ge(s_node, 1)
            dve.tensor_copy(node_hi[:, :], node_f[:, :]).then_inc(s_nodehi, 1)
            dve.tensor_scalar(node_neg[:, :], node_f[:, :], -1.0, None, ALU.mult).then_inc(s_nodeneg, 1)
            for c in range(BT + 1):
                dve.tensor_scalar(past[:, :, c], node_f[:, :], float(c * P), None, ALU.is_ge).then_inc(s_rowform, 1)
            dve.wait_ge(s_dump, 1)
            dve.tensor_tensor(node_dump[:, :].rearrange("p (m t) -> p m t", t=BT),
                              node_f[:, :].rearrange("p (m t) -> p m t", t=BT),
                              dump[:, :].unsqueeze(1).to_broadcast([P, batches, BT]),
                              ALU.subtract).then_inc(s_rowform, 1)
            dve.wait_ge(s_rowform, BT + 2)
            dve.tensor_reduce(blocks_past[:, :], past[:, :, 1:BT], AX_X, ALU.add).then_inc(s_rowform, 1)
            dve.tensor_tensor(is_low[:, :, :], past[:, :, 0:BT], past[:, :, 1:BT + 1],
                              ALU.subtract).then_inc(s_rowform, 1)
            dve.tensor_tensor(node_off[:, :], past[:, :, BT], node_dump[:, :], ALU.mult).then_inc(s_nodeoff, 1)
            dve.wait_ge(s_rowform, BT + 3)
            dve.scalar_tensor_tensor(out=node_row[:, :], in0=blocks_past[:, :], scalar=-float(P), in1=node_f[:, :],
                                     op0=ALU.mult, op1=ALU.add).then_inc(s_rowform, 1)
            dve.wait_ge(s_nodehi, 1)
            dve.tensor_tensor(node_lo[:, :], node_f[:, :], node_hi[:, :], ALU.subtract).then_inc(s_nodelo, 1)

            def spread(t):
                return t[:, :].unsqueeze(2).to_broadcast([P, BT, f])

            def tents(m, axis, n):
                return tent[:, tl(m, 0, BT), axis, :].unsqueeze(3).to_broadcast([P, BT, n, f])

            def step(s, at, r):
                norm, g = at < batches, at % SLOTS
                weigh, first_w = there(at, WEIGH)
                m, gm = s - WEIGH, (at - WEIGH) % SLOTS
                placed, first_p = there(at, COMBINE)
                if placed:
                    d = s - COMBINE
                    dve.wait_ge(s_kept, d + 1)
                    dve.wait_ge(s_room, d + 1)
                    dve.tensor_tensor(scat_idx[:, bass.ds(d % ADD_SLOTS * BT, BT)], kept[:, :], dump[:, :],
                                      ALU.add).then_inc(s_sidx, 1)
                chosen, first_k = there(at, KEEP)
                if chosen:
                    d = s - KEEP
                    dve.wait_ge(s_same, BT * (d + 1))
                    if first_k:
                        dve.wait_ge(s_nodeoff, 1)
                    else:
                        dve.wait_ge(s_sidx, d)
                    dve.scalar_tensor_tensor(out=kept[:, :], in0=count[:, :], scalar=1.0,
                                             in1=node_off[:, tl(d, 0, BT)],
                                             op0=ALU.is_equal, op1=ALU.mult).then_inc(s_kept, 1)
                if weigh:
                    dve.wait_ge(s_prod, m + 1)
                    if not first_w:
                        dve.wait_ge(s_msg, m)
                    dve.tensor_tensor(weighed[:, :, :, :], prod[:, :].rearrange("p (t b o) -> p t b o", b=n_v, o=f),
                                      tents(m, 1, n_v), ALU.mult).then_inc(s_weigh, 1)
                    dve.wait_ge(s_weigh, m + 1)
                    dve.tensor_reduce(msg[:, tl(m, 0, BT), :], weighed[:, :, :, :].rearrange("p t b o -> p t o b"),
                                      AX_X, ALU.add).then_inc(s_msg, 1)
                if norm:
                    dve.wait_ge(s_gath[g], 16 * BT * (r + at // SLOTS + 1))
                    rows = gath[:, g * BT:(g + 1) * BT, :]
                    dve.tensor_reduce(row_sum[:, :], rows, AX_X, ALU.add).then_inc(s_sum, 1)
                    dve.wait_ge(s_sum, s + 1)
                    if at > 0:
                        dve.wait_ge(s_h, s)
                    dve.scalar_tensor_tensor(out=cen[:, :, :], in0=spread(row_sum), scalar=-1.0 / f, in1=rows,
                                             op0=ALU.mult, op1=ALU.add).then_inc(s_cen, 1)
                    dve.wait_ge(s_cen, s + 1)
                    dve.tensor_tensor(cen_sq[:, :, :], cen[:, :, :], cen[:, :, :], ALU.mult).then_inc(s_sq, 1)
                    dve.wait_ge(s_sq, s + 1)
                    dve.tensor_reduce(sq_sum[:, :], cen_sq[:, :, :], AX_X, ALU.add).then_inc(s_var, 1)
                if weigh:
                    if first_w:
                        dve.wait_ge(s_rowform, BT + 5)
                        dve.wait_ge(s_column, 1)
                    dve.tensor_tensor(low_hot[:, gm, :, :], column[:, :].unsqueeze(1).to_broadcast([P, BT, P]),
                                      node_row[:, tl(m, 0, BT)].unsqueeze(2).to_broadcast([P, BT, P]),
                                      ALU.is_equal).then_inc(s_lowhot, 1)
                    dve.wait_ge(s_msg, m + 1)
                    dve.tensor_tensor(low_msg[:, gm, :, :, :],
                                      msg[:, tl(m, 0, BT), :].unsqueeze(2).to_broadcast([P, BT, BT, f]),
                                      is_low[:, tl(m, 0, BT), :].unsqueeze(3).to_broadcast([P, BT, BT, f]),
                                      ALU.mult).then_inc(s_lowmsg, 1)
                if norm:
                    dve.wait_ge(s_std, s + 1)
                    dve.reciprocal(rstd[:, :], std[:, :]).then_inc(s_rstd, 1)
                    dve.wait_ge(s_rstd, s + 1)
                    dve.scalar_tensor_tensor(out=h[:, :, :], in0=cen[:, :, :], scalar=0.0, in1=spread(rstd),
                                             op0=ALU.max, op1=ALU.mult).then_inc(s_h, 1)
                    dve.wait_ge(s_h, s + 1)
                    if at == 0:
                        dve.wait_ge(s_tent, 1)
                    else:
                        dve.wait_ge(s_turned, s)
                    dve.tensor_tensor(z[:, :, :, :], h[:, :, :].unsqueeze(2).to_broadcast([P, BT, n_u, f]),
                                      tents(s, 0, n_u), ALU.mult).then_inc(s_z, 1)

            steps(dve, step)
            dve.wait_ge(s_xlow, 16)
            dve.wait_ge(s_low, batches)
            dve.tensor_tensor(low_out[:, :, :], low[:, :].rearrange("p (c o) -> p c o", c=BT), x_low[:, :, :],
                              ALU.add).then_inc(s_low_out, 1)


_INS = ["x", "src", "dst", "edge_attr_2", "L0_gnn_weight"]


def kernel(**inputs):
    import numpy as np
    import concourse.bacc as bacc
    from concourse.bass_utils import run_bass_kernel_spmd

    nc = bacc.Bacc("TRN2", target_bir_lowering=False, num_devices=1)
    arrays, args = {}, []
    for name in _INS:
        a = np.ascontiguousarray(inputs[name])
        arrays[f"in_{name}"] = a
        args.append(nc.dram_tensor(f"in_{name}", a.shape, mybir.dt.from_np(a.dtype), kind="ExternalInput").ap())
    shape = arrays["in_x"].shape
    args.append(nc.dram_tensor("out", shape, F32, kind="ExternalOutput").ap())
    gnn_kernel(nc, *args)
    r = run_bass_kernel_spmd(nc, [arrays], core_ids=[0])
    return r.results[0]["out"]
```
